# Optimizing a Trainium2 kernel written in Bass

```python
import numpy as np
import jax
import jax.numpy as jnp

def _softmax(x, axis=-1):
    return jax.nn.softmax(x, axis=axis)

def _gelu(x):
    return jax.nn.gelu(x, approximate=True)

def _silu(x):
    return jax.nn.silu(x)

def _sigmoid(x):
    return jax.nn.sigmoid(x)

def _layernorm(x, axis=-1, eps=1e-05):
    m = jnp.mean(x, axis=axis, keepdims=True)
    v = jnp.var(x, axis=axis, keepdims=True)
    return (x - m) / jnp.sqrt(v + eps)

def _scatter_add(tgt, idx, src, axis=0):
    return tgt.at[idx].add(src)

def _segment_sum(src, seg, n):
    return jax.ops.segment_sum(src, seg, n)
kernel_name = 'mk_adj_preln_d2_adj_r2_e28244'

def setup_inputs(seed: int=0):
    np.random.seed(seed)
    _w = jnp.asarray

    def _rec_inputs():
        import jax
        import jax.numpy as jnp
        _gk = jax.random.key(seed)
        x = -0.0005146 + 1 * jax.random.normal(jax.random.fold_in(_gk, 1), (8, 1024, 128), jnp.float32)
        _w = (1.0 + jnp.arange(1024, dtype=jnp.float32)) ** (-0.5)
        _w = _w / _w.mean()
        _pij = jnp.clip(0.0078125 * _w[:, None] * _w[None, :], 0.0, 1.0)
        _a = jax.random.uniform(jax.random.fold_in(_gk, 2), (8, 1024, 1024)) < _pij
        adj = _a.astype(jnp.int32)
        return (x, adj)
    x, adj = _rec_inputs()

    def _L0_gnn_setup():
        import jax, jax.numpy as jnp
        import numpy as np
        B, N, C, OUT, S = (4, 1024, 128, 128, 25)
        DENSITY = 0.008
        key = jax.random.key(seed)
        kA, kX, kW = jax.random.split(key, 3)
        A = jax.random.bernoulli(kA, DENSITY, (B, N, N)).astype(jnp.int32)
        X = jax.random.normal(kX, (B, N, C), dtype=jnp.float32)
        W = jax.random.normal(kW, (2 * C, OUT), dtype=jnp.float32) * np.float32(1.0 / np.sqrt(2 * C))
        b = jnp.zeros((OUT,), dtype=jnp.float32)
        return {'A': A, 'X': X, 'W': W, 'b': b}
    _L0_gnn_all = _L0_gnn_setup()
    _L0_gnn_in = {k: v for k, v in _L0_gnn_all.items() if k in ('W', 'b')}
    del _L0_gnn_all

    def _L1_gnn_setup():
        import jax, jax.numpy as jnp
        import numpy as np
        LEAKY_SLOPE = 0.2
        NEG_INF = -9000000000000000.0

        def _edge_scores(h, a_k):
            e = jnp.einsum('bid,bjd->bij', h * a_k[:, 0], h)
            return jax.nn.leaky_relu(e, negative_slope=LEAKY_SLOPE)
        key = jax.random.key(seed)
        k1, k2, k3, k4, k5, k6 = jax.random.split(key, 6)
        B, N, D = (32, 256, 128)
        hidden = jax.random.normal(k1, (B, N, D), dtype=jnp.float32)
        adj = jax.random.randint(k2, (B, N, N), 0, 5, dtype=jnp.int32)
        a_0 = jax.random.normal(k3, (D, 1), dtype=jnp.float32)
        a_1 = jax.random.normal(k4, (D, 1), dtype=jnp.float32)
        a_2 = jax.random.normal(k5, (D, 1), dtype=jnp.float32)
        a_3 = jax.random.normal(k6, (D, 1), dtype=jnp.float32)
        return {'hidden': hidden, 'adj': adj, 'a_0': a_0, 'a_1': a_1, 'a_2': a_2, 'a_3': a_3}
    _L1_gnn_all = _L1_gnn_setup()
    _L1_gnn_in = {k: v for k, v in _L1_gnn_all.items() if k in ('a_0', 'a_1', 'a_2', 'a_3')}
    del _L1_gnn_all
    return {'x': x, 'adj': adj, 'L0_gnn_W': _L0_gnn_in['W'], 'L0_gnn_b': _L0_gnn_in['b'], 'L1_gnn_a_0': _L1_gnn_in['a_0'], 'L1_gnn_a_1': _L1_gnn_in['a_1'], 'L1_gnn_a_2': _L1_gnn_in['a_2'], 'L1_gnn_a_3': _L1_gnn_in['a_3']}

def reference(x, adj, L0_gnn_W, L0_gnn_b, L1_gnn_a_0, L1_gnn_a_1, L1_gnn_a_2, L1_gnn_a_3):
    import jax
    import jax.numpy as jnp

    def _L0_gnn_ref(A, X, W, b):
        import jax, jax.numpy as jnp
        import numpy as np
        B, N, C, OUT, S = (4, 1024, 128, 128, 25)
        DENSITY = 0.008
        mask = A != 0
        neg_inf = jnp.float32(-jnp.inf)
        pri = -jnp.arange(N, dtype=jnp.float32)
        scores = jnp.where(mask, pri, neg_inf)
        vals, idx = jax.lax.top_k(scores, S)
        valid = vals > neg_inf
        feats = jax.vmap(lambda x, i: x[i])(X, idx)
        feats = jnp.where(valid[..., None], feats, neg_inf)
        agg = feats.max(axis=2)
        degree = mask.sum(axis=-1)
        agg = jnp.where((degree <= S)[..., None], jnp.maximum(agg, 0.0), agg)
        h = jnp.concatenate([X, agg], axis=-1)
        out = jax.nn.relu(jnp.einsum('bnf,fo->bno', h, W) + b)
        return out

    def _L1_gnn_ref(hidden, adj, a_0, a_1, a_2, a_3):
        import jax, jax.numpy as jnp
        import numpy as np
        LEAKY_SLOPE = 0.2
        NEG_INF = -9000000000000000.0

        def _edge_scores(h, a_k):
            e = jnp.einsum('bid,bjd->bij', h * a_k[:, 0], h)
            return jax.nn.leaky_relu(e, negative_slope=LEAKY_SLOPE)
        h = hidden
        e_0 = _edge_scores(h, a_0)
        e_1 = _edge_scores(h, a_1)
        e_2 = _edge_scores(h, a_2)
        e_3 = _edge_scores(h, a_3)
        scores = jnp.where(adj == 1, e_0, NEG_INF)
        scores = jnp.where(adj == 2, e_1, scores)
        scores = jnp.where(adj == 3, e_2, scores)
        scores = jnp.where(adj == 4, e_3, scores)
        alpha = jax.nn.softmax(scores, axis=-1)
        return jnp.einsum('bij,bjd->bid', alpha, h)
    h = jnp.maximum(_layernorm(x, axis=-1), 0.0)
    x = x + _L0_gnn_ref(adj, h, L0_gnn_W, L0_gnn_b)
    h = jnp.maximum(_layernorm(x, axis=-1), 0.0)
    x = x + _L1_gnn_ref(h, adj, L1_gnn_a_0, L1_gnn_a_1, L1_gnn_a_2, L1_gnn_a_3)
    return x

_drawn_inputs = setup_inputs


def setup_inputs(seed=0):
    import zlib

    import numpy as np

    out = dict(_drawn_inputs(seed))
    spreads = {'L0_gnn_b': (0.0, 0.1)}
    factors = {}
    for name, (base, spread) in spreads.items():
        noise = np.random.default_rng([zlib.crc32(name.encode()), seed]).standard_normal(out[name].shape)
        drawn = base * np.exp(spread * noise) if base else spread * noise
        out[name] = jnp.asarray(drawn.astype(out[name].dtype))
    for name, factor in factors.items():
        out[name] = (out[name] * factor).astype(out[name].dtype)
    return out
```

```python
from contextlib import ExitStack

import concourse.bass as bass
from concourse import mybir

GRAPHS, NODES, CHANNELS = 8, 1024, 128
P = 128
TILES = NODES // P
HALF = NODES // 2
NEIGHBOURS = 25
EDGE_TYPES = 4
EPS = 1e-5
SLOPE = 0.2
MASKED = -9000000000000000.0
FP16_SCALE = 4096.0
BIG = 3.0e38


def program(nc, x, adj, w, bias, a_list, out):
    f32, bf16, fp16, i32, u16 = (mybir.dt.float32, mybir.dt.bfloat16, mybir.dt.float16,
                                 mybir.dt.int32, mybir.dt.uint16)
    ALU, ACT = mybir.AluOpType, mybir.ActivationFunctionType

    with ExitStack() as ctx:
        def sb(name, shape, dt):
            return ctx.enter_context(nc.sbuf_tensor(name, shape, dt))

        def sem(name):
            return ctx.enter_context(nc.semaphore(name))

        adj_in = sb("adj_in", [P, TILES, NODES], i32)
        x_in = sb("x_in", [P, TILES, CHANNELS], f32)
        w_sb = sb("w_sb", [P, 2, CHANNELS], f32)
        w_agg = sb("w_agg", [P, CHANNELS], f32)
        bias_sb = sb("bias_sb", [1, CHANNELS], f32)
        a_sb = sb("a_sb", [P, EDGE_TYPES], f32)
        ones_row = sb("ones_row", [1, P], f32)
        ident_f = sb("ident_f", [P, P], f32)
        ident_b = sb("ident_b", [P, P], bf16)
        upto = sb("upto", [P, P], bf16)
        all_ones = sb("all_ones", [P, P], bf16)
        slot_no = sb("slot_no", [P, 32], f32)
        adj_c = sb("adj_c", [P, TILES, NODES], bf16)
        mask_t = sb("mask_t", [P, TILES, NODES], bf16)
        before = sb("before", [P, 2, NODES], bf16)
        rank = sb("rank", [P, TILES, NODES], fp16)
        pick = sb("pick", [P, 2, TILES, HALF], fp16)
        h = sb("h", [P, TILES, CHANNELS], f32)
        h_hi = sb("h_hi", [P, TILES, CHANNELS], fp16)
        h_lo = sb("h_lo", [P, TILES, CHANNELS], fp16)
        h_t = sb("h_t", [P, NODES], f32)
        agg = sb("agg", [P, NODES], f32)
        stats = sb("stats", [P, TILES, 6], f32)
        mean_var = sb("mean_var", [P, TILES, 2], f32)
        var_eps = sb("var_eps", [P, TILES], f32)
        rstd = sb("rstd", [P, TILES], f32)
        minus_half = sb("minus_half", [P, TILES], f32)
        x1 = sb("x1", [P, TILES, CHANNELS], f32)
        ah_t = sb("ah_t", [P, EDGE_TYPES, NODES], f32)
        type_mask = sb("type_mask", [P, 2, NODES], u16)
        score = sb("score", [P, 3, NODES], f32)
        relu4 = sb("relu4", [P, 2, NODES], f32)
        prob = sb("prob", [P, 2, NODES], f32)
        prob_t = sb("prob_t", [P, 2, TILES, P], f32)
        neg_max = sb("neg_max", [P, TILES], f32)
        row_sum = sb("row_sum", [P, TILES], f32)
        inv_sum = sb("inv_sum", [P, TILES], f32)
        y = sb("y", [P, TILES, CHANNELS], f32)

        ps_a = [ctx.enter_context(nc.psum_tensor(f"ps_a{i}", [P, NODES], f32)) for i in range(2)]
        ps_b = [ctx.enter_context(nc.psum_tensor(f"ps_b{i}", [P, NODES], f32)) for i in range(2)]
        ps_mask = [t[:, 0:HALF].bitcast(bf16) for t in ps_a]
        ps_b3 = [t[:, :].rearrange("p (t c) -> p t c", t=TILES) for t in ps_b]

        weights_loaded = sem("weights_loaded")
        adj_loaded = sem("adj_loaded")
        x_loaded = sem("x_loaded")
        out_stored = sem("out_stored")
        fill_done = sem("fill_done")
        consts_ready = sem("consts_ready")
        w_scaled = sem("w_scaled")
        adjc_ready = sem("adjc_ready")
        var_ready = sem("var_ready")
        rstd_ready = sem("rstd_ready")
        h_ready = sem("h_ready")
        maskt_full = sem("maskt_full")
        maskt_ready = sem("maskt_ready")
        before_ready = sem("before_ready")
        count_full = sem("count_full")
        rank_ready = sem("rank_ready")
        ht_full = sem("ht_full")
        ht_ready = sem("ht_ready")
        pick_ready = [sem(f"pick_ready{i}") for i in range(2)]
        gather_full = [sem(f"gather_full{i}") for i in range(2)]
        agg_done = [sem(f"agg_done{i}") for i in range(2)]
        lin_full = sem("lin_full")
        x1_ready = sem("x1_ready")
        h2_ready = sem("h2_ready")
        h2t_full = sem("h2t_full")
        ah_ready = sem("ah_ready")
        e_full = sem("e_full")
        e_used = sem("e_used")
        score_filled = sem("score_filled")
        type_ready = sem("type_ready")
        relu_ready = sem("relu_ready")
        logit_ready = sem("logit_ready")
        prob_ready = sem("prob_ready")
        pt_full = sem("pt_full")
        pt_ready = sem("pt_ready")
        pv_full = sem("pv_full")
        y_ready = sem("y_ready")
        dve_step = sem("dve_step")
        E_USES = TILES * EDGE_TYPES

        block = ctx.enter_context(nc.Block())

        @block.sync
        def _(sp):
            sp.dma_start(w_sb[:], w.rearrange("(t p) c -> p t c", p=P)).then_inc(weights_loaded, 16)
            sp.dma_start(bias_sb[:], bias).then_inc(weights_loaded, 16)
            for k in range(EDGE_TYPES):
                sp.dma_start(a_sb[:, k:k + 1], a_list[k]).then_inc(weights_loaded, 16)
            def load(b):
                sp.dma_start(x_in[:], x[b].rearrange("(t p) c -> p t c", p=P)).then_inc(x_loaded, 16)
                sp.dma_start(adj_in[:], adj[b].rearrange("(t p) j -> p t j", p=P)).then_inc(adj_loaded, 16)

            load(0)
            with sp.Fori(1, GRAPHS) as b:
                sp.wait_ge(adjc_ready, b * TILES)
                sp.wait_ge(x1_ready, b)
                load(b)
            sp.wait_ge(out_stored, 16 * (1 + TILES * GRAPHS))

        @block.gpsimd
        def _(pool):
            read = pool.alloc_register("read")
            nc.gpsimd.memset(ident_f[:], 0.0)
            nc.gpsimd.memset(upto[:], 1.0)
            nc.gpsimd.memset(all_ones[:], 1.0)
            nc.gpsimd.memset(ones_row[:], 1.0)
            nc.gpsimd.memset(minus_half[:], -0.5)
            nc.gpsimd.iota(slot_no[:], pattern=[[1, 32]], base=1, channel_multiplier=0,
                           allow_small_or_imprecise_dtypes=True).then_inc(fill_done, 1)
            pool.wait_ge(fill_done, 1)
            nc.gpsimd.affine_select(out=ident_f[:], in_=ident_f[:], compare_op=ALU.not_equal, fill=1.0,
                                    base=0, pattern=[[-1, P]], channel_multiplier=1)
            nc.gpsimd.affine_select(out=upto[:], in_=upto[:], compare_op=ALU.is_ge, fill=0.0,
                                    base=0, pattern=[[1, P]], channel_multiplier=-1).then_inc(fill_done, 1)
            pool.wait_ge(fill_done, 2)
            nc.gpsimd.tensor_copy(ident_b[:], ident_f[:]).then_inc(consts_ready, 1)
            with pool.Fori(0, GRAPHS) as b:
                for layer in range(2):
                    pool.wait_ge(var_ready, b * 2 + layer + 1)
                    nc.gpsimd.tensor_tensor(rstd[:], var_eps[:], minus_half[:], ALU.pow).then_inc(rstd_ready, 1)
                for it in range(TILES):
                    if it >= 3:
                        pool.reg_mov(read, b * TILES + it - 2)
                        pool.wait_ge(consts_ready, 1)
                        pool.wait_ge(logit_ready, read)
                    nc.gpsimd.memset(score[:, it % 3, :], MASKED / SLOPE).then_inc(score_filled, 1)

        @block.scalar
        def _(act):
            act.wait_ge(weights_loaded, 16 * 6)
            act.sem_inc(out_stored, 16)
            with act.Fori(0, GRAPHS) as b:
                act.wait_ge(adj_loaded, b * 16 + 16)
                for it in range(TILES):
                    nc.scalar.activation(adj_c[:, it, :], adj_in[:, it, :], ACT.Copy).then_inc(adjc_ready, 1)
                act.wait_ge(ht_full, b + 1)
                nc.scalar.activation(h_t[:], ps_b[0][:], ACT.Copy).then_inc(ht_ready, 1)
                act.wait_ge(h2t_full, b + 1)
                nc.scalar.activation(h_t[:], ps_b[0][:], ACT.Copy).then_inc(ah_ready, 1)
                for k in range(EDGE_TYPES):
                    nc.scalar.activation(ah_t[:, k, :], ps_b[0][:], ACT.Copy,
                                         scale=a_sb[:, k:k + 1]).then_inc(ah_ready, 1)
                for step in range(TILES + 3):
                    it = step
                    if it < TILES:
                        act.wait_ge(e_used, b * E_USES + EDGE_TYPES * (it + 1))
                        nc.scalar.activation(relu4[:, it % 2, :], score[:, it % 3, :], ACT.Relu,
                                             scale=1.0 / SLOPE - 1.0).then_inc(relu_ready, 1)
                    it = step - 1
                    if 0 <= it < TILES:
                        act.wait_ge(logit_ready, b * TILES + it + 1)
                        nc.scalar.activation(prob[:, it % 2, :], relu4[:, it % 2, :], ACT.Exp, scale=-1.0,
                                             bias=neg_max[:, it:it + 1],
                                             accum_out=row_sum[:, it:it + 1]).then_inc(prob_ready, 1)
                        act.wait_ge(pt_full, b * TILES + it + 1)
                        nc.scalar.activation(prob_t[:, it % 2], ps_b3[0], ACT.Copy).then_inc(pt_ready, 1)
                    it = step - 3
                    if it >= 0:
                        act.wait_ge(y_ready, b * TILES + it + 1)
                        act.dma_start(out[b, it * P:(it + 1) * P, :], y[:, it, :]).then_inc(out_stored, 16)

        @block.vector
        def _(dve):
            STEPS = 2 * 3 + 1 + TILES
            steps = [0]
            apart = dve.alloc_register("apart")
            dve.wait_ge(weights_loaded, 16 * 6)
            nc.vector.tensor_scalar(w_agg[:], w_sb[:, 1, :], 1.0 / FP16_SCALE, None,
                                    ALU.mult).then_inc(w_scaled, 1)
            dve.wait_ge(consts_ready, 1)

            def link(b, instruction):
                instruction.then_inc(dve_step, 1)
                steps[0] += 1
                dve.wait_ge(dve_step, b * STEPS + steps[0])

            def value_apart(value):
                dve.reg_mov(apart, value)
                dve.wait_ge(consts_ready, 1)
                return apart

            def norm(b, src, layer):
                for t in range(TILES):
                    last = nc.vector.bn_stats(stats[:, t, :], src[:, t, :])
                last.then_inc(dve_step, 1)
                steps[0] += 1
                dve.wait_ge(dve_step, value_apart(b * STEPS + steps[0]))
                for t in range(TILES):
                    last = nc.vector.bn_aggr(mean_var[:, t, :], stats[:, t, :])
                link(b, last)
                nc.vector.tensor_scalar(var_eps[:], mean_var[:, :, 1], EPS, None, ALU.add).then_inc(var_ready, 1)
                dve.wait_ge(rstd_ready, b * 2 + layer + 1)
                for t in range(TILES):
                    last = nc.vector.tensor_scalar(h[:, t, :], src[:, t, :], mean_var[:, t, 0:1],
                                                   rstd[:, t:t + 1], ALU.subtract, ALU.mult)
                link(b, last)

            def make_pick(s, half):
                nc.vector.tensor_scalar(pick[:, half], rank[:, :, half * HALF:(half + 1) * HALF],
                                        slot_no[:, bass.ds(s, 1)], None,
                                        ALU.is_equal).then_inc(pick_ready[half], 1)

            def take_max(b, s, half):
                cols = slice(half * HALF, (half + 1) * HALF)
                dve.wait_ge(gather_full[half], b * NEIGHBOURS + s + 1)
                dve.wait_ge(agg_done[half], b * (NEIGHBOURS + 1) + s + 1)
                nc.vector.tensor_tensor(agg[:, cols], ps_a[half][:, 0:HALF], agg[:, cols],
                                        ALU.max).then_inc(agg_done[half], 1)

            with dve.Fori(0, GRAPHS) as b:
                steps[0] = 0
                dve.wait_ge(x_loaded, b * 16 + 16)
                norm(b, x_in, 0)
                nc.vector.tensor_scalar(h_hi[:], h[:], 0.0, FP16_SCALE, ALU.max, ALU.mult)
                link(b, nc.vector.tensor_scalar(h[:], h[:], 0.0, None, ALU.max))
                nc.vector.scalar_tensor_tensor(h_lo[:], h[:], FP16_SCALE, h_hi[:], ALU.mult,
                                               ALU.subtract).then_inc(h_ready, 1)
                for t in range(TILES + 1):
                    if t < TILES:
                        dve.wait_ge(maskt_full, b * TILES + t + 1)
                        nc.vector.tensor_scalar(mask_t[:, t, :], ps_mask[t % 2], 0.0, None,
                                                ALU.not_equal).then_inc(maskt_ready, 1)
                    if t >= 1:
                        dve.wait_ge(count_full, b * TILES + t)
                        nc.vector.tensor_tensor(rank[:, t - 1, :], ps_b[(t - 1) % 2][:], mask_t[:, t - 1, :],
                                                ALU.mult).then_inc(rank_ready, 1)
                    if t < TILES - 1:
                        dve.wait_ge(maskt_ready, b * TILES + t + 1)
                        if t == 0:
                            nc.vector.tensor_copy(before[:, 1, :], mask_t[:, 0, :]).then_inc(before_ready, 1)
                        else:
                            dve.wait_ge(before_ready, b * (TILES - 1) + t)
                            nc.vector.tensor_tensor(before[:, (t + 1) % 2, :], before[:, t % 2, :],
                                                    mask_t[:, t, :], ALU.add).then_inc(before_ready, 1)
                dve.wait_ge(rank_ready, b * TILES + TILES)
                for half in range(2):
                    nc.vector.memset(agg[:, half * HALF:(half + 1) * HALF], 0.0).then_inc(agg_done[half], 1)
                for half in range(2):
                    make_pick(0, half)
                with dve.Fori(0, NEIGHBOURS - 1) as s:
                    for half in range(2):
                        take_max(b, s, half)
                        make_pick(s + 1, half)
                for half in range(2):
                    take_max(b, NEIGHBOURS - 1, half)
                dve.wait_ge(lin_full, b + 1)
                nc.vector.scalar_tensor_tensor(x1[:], ps_b3[1], 0.0, x_in[:], ALU.max,
                                               ALU.add).then_inc(x1_ready, 1)
                dve.wait_ge(x1_ready, b + 1)
                norm(b, x1, 1)
                nc.vector.tensor_scalar(h[:], h[:], 0.0, None, ALU.max).then_inc(h2_ready, 1)
                for step in range(TILES + 2):
                    it = step
                    if it < TILES:
                        dve.wait_ge(score_filled, b * TILES + it + 1)
                        for k in range(EDGE_TYPES):
                            use = it * EDGE_TYPES + k
                            if use >= 2:
                                dve.wait_ge(e_used, b * E_USES + use - 1)
                            nc.vector.tensor_scalar(type_mask[:, k % 2, :], adj_c[:, it, :], float(k + 1), None,
                                                    ALU.is_equal).then_inc(type_ready, 1)
                            chosen = value_apart(b * E_USES + use + 1)
                            dve.wait_ge(type_ready, chosen)
                            dve.wait_ge(e_full, chosen)
                            nc.vector.copy_predicated(score[:, it % 3, :], type_mask[:, k % 2, :],
                                                      ps_a[use % 2][:]).then_inc(e_used, 1)
                    it = step - 1
                    if 0 <= it < TILES:
                        dve.wait_ge(relu_ready, value_apart(b * TILES + it + 1))
                        nc.vector.tensor_tensor_reduce(out=relu4[:, it % 2, :], in0=score[:, it % 3, :],
                                                       in1=relu4[:, it % 2, :], scale=-SLOPE, scalar=BIG,
                                                       op0=ALU.add, op1=ALU.min,
                                                       accum_out=neg_max[:, it:it + 1]).then_inc(logit_ready, 1)
                    it = step - 2
                    if it >= 0:
                        dve.wait_ge(prob_ready, b * TILES + it + 1)
                        link(b, nc.vector.reciprocal(inv_sum[:, it:it + 1], row_sum[:, it:it + 1]))
                        dve.wait_ge(pv_full, b * TILES + it + 1)
                        dve.wait_ge(out_stored, b * (16 * TILES) + 16)
                        nc.vector.scalar_tensor_tensor(y[:, it, :], ps_b[1][:, 0:CHANNELS], inv_sum[:, it:it + 1],
                                                       x1[:, it, :], ALU.mult, ALU.add).then_inc(y_ready, 1)
                assert steps[0] == STEPS, steps

        @block.tensor
        def _(pe):
            def cols(half):
                return slice(half * HALF, (half + 1) * HALF)

            def count_edges(b, t):
                pe.wait_ge(maskt_ready, b * TILES + t + 1)
                if t >= 1:
                    pe.wait_ge(before_ready, b * (TILES - 1) + t)
                if t >= 2:
                    pe.wait_ge(rank_ready, b * TILES + t - 1)
                for half in range(2):
                    last = nc.tensor.matmul(ps_b[t % 2][:, cols(half)], upto[:], mask_t[:, t, cols(half)],
                                            start=True, stop=(t == 0))
                for half in range(2 if t else 0):
                    last = nc.tensor.matmul(ps_b[t % 2][:, cols(half)], all_ones[:], before[:, t % 2, cols(half)],
                                            start=False, stop=True)
                last.then_inc(count_full, 1)

            def gather(b, s, half):
                pe.wait_ge(pick_ready[half], b * NEIGHBOURS + s + 1)
                pe.wait_ge(agg_done[half], b * (NEIGHBOURS + 1) + s + 1)
                for t in range(TILES):
                    for part in (h_hi, h_lo):
                        last = nc.tensor.matmul(ps_a[half][:, 0:HALF], part[:, t, :], pick[:, half, t, :],
                                                start=(t == 0 and part is h_hi),
                                                stop=(t == TILES - 1 and part is h_lo))
                last.then_inc(gather_full[half], 1)

            def scores(b, use):
                it, k = divmod(use, EDGE_TYPES)
                if it == 0:
                    pe.wait_ge(ah_ready, b * (1 + EDGE_TYPES) + 2 + k)
                if use >= 2:
                    pe.wait_ge(e_used, b * E_USES + use - 1)
                for half in range(2):
                    last = nc.tensor.matmul(ps_a[use % 2][:, cols(half)], ah_t[:, k, it * P:(it + 1) * P],
                                            h_t[:, cols(half)], start=True, stop=True)
                last.then_inc(e_full, 1)

            pe.wait_ge(consts_ready, 1)
            pe.wait_ge(w_scaled, 1)
            with pe.Fori(0, GRAPHS) as b:
                for t in range(TILES + 1):
                    if t < TILES:
                        if t == 0:
                            pe.wait_ge(adjc_ready, b * TILES + TILES)
                        if t >= 2:
                            pe.wait_ge(maskt_ready, b * TILES + t - 1)
                        for it in range(TILES):
                            last = nc.tensor.transpose(ps_mask[t % 2][:, it * P:(it + 1) * P],
                                                       adj_c[:, it, t * P:(t + 1) * P], ident_b[:])
                        last.then_inc(maskt_full, 1)
                    if t >= 1:
                        count_edges(b, t - 1)
                pe.wait_ge(h_ready, b + 1)
                pe.wait_ge(rank_ready, b * TILES + TILES)
                for t in range(TILES):
                    last = nc.tensor.transpose(ps_b3[0][:, t, :], h[:, t, :], ident_f[:])
                last.then_inc(ht_full, 1)
                with pe.Fori(0, NEIGHBOURS) as s:
                    for half in range(2):
                        gather(b, s, half)
                pe.wait_ge(ht_ready, b + 1)
                for half in range(2):
                    pe.wait_ge(agg_done[half], (b + 1) * (NEIGHBOURS + 1))
                for t in range(TILES):
                    rows = slice(t * P, (t + 1) * P)
                    nc.tensor.matmul(ps_b3[1][:, t, :], h_t[:, rows], w_sb[:, 0, :], start=True, stop=False)
                    nc.tensor.matmul(ps_b3[1][:, t, :], agg[:, rows], w_agg[:], start=False, stop=False)
                    last = nc.tensor.matmul(ps_b3[1][:, t, :], ones_row[:], bias_sb[:], start=False, stop=True)
                last.then_inc(lin_full, 1)
                pe.wait_ge(h2_ready, b + 1)
                for t in range(TILES):
                    last = nc.tensor.transpose(ps_b3[0][:, t, :], h[:, t, :], ident_f[:])
                last.then_inc(h2t_full, 1)
                for use in range(2):
                    scores(b, use)
                for step in range(TILES + 1):
                    for use in range(step * EDGE_TYPES + 2, min(step * EDGE_TYPES + 6, E_USES)):
                        scores(b, use)
                    it = step - 1
                    if it >= 0:
                        pe.wait_ge(prob_ready, b * TILES + it + 1)
                        if it >= 1:
                            pe.wait_ge(pt_ready, b * TILES + it)
                        for t in range(TILES):
                            last = nc.tensor.transpose(ps_b3[0][:, t, :], prob[:, it % 2, t * P:(t + 1) * P],
                                                       ident_f[:])
                        last.then_inc(pt_full, 1)
                        pe.wait_ge(pt_ready, b * TILES + it + 1)
                        if it >= 1:
                            pe.wait_ge(y_ready, b * TILES + it)
                        for t in range(TILES):
                            last = nc.tensor.matmul(ps_b[1][:, 0:CHANNELS], prob_t[:, it % 2, t, :], h[:, t, :],
                                                    start=(t == 0), stop=(t == TILES - 1))
                        last.then_inc(pv_full, 1)


def kernel(x, adj, L0_gnn_W, L0_gnn_b, L1_gnn_a_0, L1_gnn_a_1, L1_gnn_a_2, L1_gnn_a_3):
    import numpy as np
    import concourse.bacc as bacc
    from concourse.bass_utils import run_bass_kernel_spmd

    nc = bacc.Bacc("TRN2", target_bir_lowering=False, num_devices=1)
    given = {"x": x, "adj": adj, "w": L0_gnn_W, "bias": np.asarray(L0_gnn_b)[None, :],
             "a0": L1_gnn_a_0, "a1": L1_gnn_a_1, "a2": L1_gnn_a_2, "a3": L1_gnn_a_3}
    arrays, aps = {}, {}
    for name, value in given.items():
        value = np.ascontiguousarray(value)
        arrays[name] = value
        aps[name] = nc.dram_tensor(name, value.shape, mybir.dt.from_np(value.dtype), kind="ExternalInput").ap()
    out = nc.dram_tensor("out", (GRAPHS, NODES, CHANNELS), mybir.dt.float32, kind="ExternalOutput").ap()
    program(nc, aps["x"], aps["adj"], aps["w"], aps["bias"], [aps[f"a{k}"] for k in range(EDGE_TYPES)], out)
    result = run_bass_kernel_spmd(nc, [arrays], core_ids=[0])
    return result.results[0]["out"]
```
